# Optimizing a Trainium2 kernel written in Bass

```python
import numpy as np
import jax
import jax.numpy as jnp

def _softmax(x, axis=-1):
    return jax.nn.softmax(x, axis=axis)

def _gelu(x):
    return jax.nn.gelu(x, approximate=True)

def _silu(x):
    return jax.nn.silu(x)

def _sigmoid(x):
    return jax.nn.sigmoid(x)

def _layernorm(x, axis=-1, eps=1e-05):
    m = jnp.mean(x, axis=axis, keepdims=True)
    v = jnp.var(x, axis=axis, keepdims=True)
    return (x - m) / jnp.sqrt(v + eps)

def _scatter_add(tgt, idx, src, axis=0):
    return tgt.at[idx].add(src)

def _segment_sum(src, seg, n):
    return jax.ops.segment_sum(src, seg, n)
kernel_name = 'mk_prb_d1_jaxref_r8_f7c910'

def setup_inputs(seed: int=0):
    np.random.seed(seed)
    _w = jnp.asarray

    def _L0_attn_setup():
        import jax, jax.numpy as jnp
        import numpy as np
        HIDDEN = 256
        HEADS = 16
        HEAD_DIM = HIDDEN // HEADS
        SCALE = 1.0 / float(np.sqrt(HEAD_DIM))
        B, S = (2, 256)
        key = jax.random.key(seed)
        ks = jax.random.split(key, 5)
        return {'x': jax.random.normal(ks[0], (B, S, HIDDEN), dtype=jnp.float32), 'q_w': jax.random.normal(ks[1], (HIDDEN, HIDDEN), dtype=jnp.float32) * HIDDEN ** (-0.5), 'k_w': jax.random.normal(ks[2], (HEAD_DIM, HIDDEN), dtype=jnp.float32) * HIDDEN ** (-0.5), 'v_w': jax.random.normal(ks[3], (HEAD_DIM, HIDDEN), dtype=jnp.float32) * HIDDEN ** (-0.5), 'o_w': jax.random.normal(ks[4], (HIDDEN, HIDDEN), dtype=jnp.float32) * HIDDEN ** (-0.5)}
    _L0_attn_in = _L0_attn_setup()

    def _L0_ffn_setup():
        import jax, jax.numpy as jnp
        import numpy as np
        TOP_K = 4
        key = jax.random.key(seed)
        ks = jax.random.split(key, 9)
        B, T, D, H, NE = (2, 128, 256, 176, 16)
        s = 0.02
        return {'x': jax.random.normal(ks[0], (B, T, D), jnp.float32), 'gate_w': jax.random.normal(ks[1], (NE, D), jnp.float32) * s, 'gate_b': jax.random.normal(ks[2], (NE,), jnp.float32) * s, 'w1_shared': jax.random.normal(ks[3], (D, H), jnp.float32) * s, 'w2_shared': jax.random.normal(ks[4], (H, D), jnp.float32) * s, 'w3_shared': jax.random.normal(ks[5], (D, H), jnp.float32) * s, 'w1_routed': jax.random.normal(ks[6], (NE, D, H), jnp.float32) * s, 'w2_routed': jax.random.normal(ks[7], (NE, H, D), jnp.float32) * s, 'w3_routed': jax.random.normal(ks[8], (NE, D, H), jnp.float32) * s}
    _L0_ffn_in = _L0_ffn_setup()
    _d = {'L0_attn_x': _L0_attn_in['x'], 'L0_attn_q_w': _L0_attn_in['q_w'], 'L0_attn_k_w': _L0_attn_in['k_w'], 'L0_attn_v_w': _L0_attn_in['v_w'], 'L0_attn_o_w': _L0_attn_in['o_w'], 'L0_ffn_gate_w': _L0_ffn_in['gate_w'], 'L0_ffn_gate_b': _L0_ffn_in['gate_b'], 'L0_ffn_w1_shared': _L0_ffn_in['w1_shared'], 'L0_ffn_w2_shared': _L0_ffn_in['w2_shared'], 'L0_ffn_w3_shared': _L0_ffn_in['w3_shared'], 'L0_ffn_w1_routed': _L0_ffn_in['w1_routed'], 'L0_ffn_w2_routed': _L0_ffn_in['w2_routed'], 'L0_ffn_w3_routed': _L0_ffn_in['w3_routed']}
    _x0 = _d['L0_attn_x']
    _d['L0_attn_x'] = jax.random.normal(jax.random.fold_in(jax.random.key(seed), 1), (2, 1024, 256), dtype=_x0.dtype)
    del _x0
    return _d

def reference(L0_attn_x, L0_attn_q_w, L0_attn_k_w, L0_attn_v_w, L0_attn_o_w, L0_ffn_gate_w, L0_ffn_gate_b, L0_ffn_w1_shared, L0_ffn_w2_shared, L0_ffn_w3_shared, L0_ffn_w1_routed, L0_ffn_w2_routed, L0_ffn_w3_routed):

    def _L0_attn_ref(x, q_w, k_w, v_w, o_w):
        import jax, jax.numpy as jnp
        import numpy as np
        HIDDEN = 256
        HEADS = 16
        HEAD_DIM = HIDDEN // HEADS
        SCALE = 1.0 / float(np.sqrt(HEAD_DIM))
        B, S = (2, 256)
        b, s, _ = x.shape
        q = (x @ q_w.T).reshape(b, s, HEADS, HEAD_DIM).transpose(0, 2, 1, 3)
        k = x @ k_w.T
        v = x @ v_w.T
        scores = jnp.einsum('bhqd,bkd->bhqk', q, k) * SCALE
        attn = jax.nn.softmax(scores.astype(jnp.float32), axis=-1).astype(q.dtype)
        out = jnp.einsum('bhqk,bkd->bhqd', attn, v)
        out = out.transpose(0, 2, 1, 3).reshape(b, s, HIDDEN)
        return out @ o_w.T

    def _L0_ffn_ref(x, gate_w, gate_b, w1_shared, w2_shared, w3_shared, w1_routed, w2_routed, w3_routed):
        import jax, jax.numpy as jnp
        import numpy as np
        TOP_K = 4
        n_experts = w1_routed.shape[0]
        logits = jnp.einsum('ed,btd->bte', gate_w, x)
        scores = jax.nn.sigmoid(logits) + gate_b
        weights, indices = jax.lax.top_k(scores, TOP_K)
        weights = weights / weights.sum(-1, keepdims=True)
        shared_out = jax.nn.silu(x @ w1_shared) * (x @ w3_shared) @ w2_shared
        one_hot = jax.nn.one_hot(indices, n_experts, dtype=x.dtype)
        router_probs = (weights[..., None] * one_hot).sum(-2)
        h1 = jnp.einsum('btd,edc->btec', x, w1_routed)
        h2 = jnp.einsum('btd,edc->btec', x, w3_routed)
        h3 = jax.nn.silu(h1 * h2)
        experts_out = jnp.einsum('btec,ecd->bted', h3, w2_routed)
        routed_out = jnp.einsum('bted,bte->btd', experts_out, router_probs)
        return shared_out + routed_out
    x = L0_attn_x
    xn = _layernorm(x, axis=-1)
    x = x + _L0_attn_ref(xn, L0_attn_q_w, L0_attn_k_w, L0_attn_v_w, L0_attn_o_w) + _L0_ffn_ref(xn, L0_ffn_gate_w, L0_ffn_gate_b, L0_ffn_w1_shared, L0_ffn_w2_shared, L0_ffn_w3_shared, L0_ffn_w1_routed, L0_ffn_w2_routed, L0_ffn_w3_routed)
    return x

_drawn_inputs = setup_inputs


def setup_inputs(seed=0):
    import zlib

    import numpy as np

    out = dict(_drawn_inputs(seed))
    spreads = {}
    factors = {'L0_ffn_gate_w': 8.0,
     'L0_ffn_gate_b': 8.0,
     'L0_ffn_w1_shared': 4.096,
     'L0_ffn_w2_shared': 4.045,
     'L0_ffn_w3_shared': 4.038,
     'L0_ffn_w1_routed': 8.0,
     'L0_ffn_w2_routed': 8.0,
     'L0_ffn_w3_routed': 8.0,
     'L0_attn_q_w': 3.573,
     'L0_attn_k_w': 3.385,
     'L0_attn_v_w': 3.16,
     'L0_attn_o_w': 3.142}
    for name, (base, spread) in spreads.items():
        noise = np.random.default_rng([zlib.crc32(name.encode()), seed]).standard_normal(out[name].shape)
        drawn = base * np.exp(spread * noise) if base else spread * noise
        out[name] = jnp.asarray(drawn.astype(out[name].dtype))
    for name, factor in factors.items():
        out[name] = (out[name] * factor).astype(out[name].dtype)
    return out
```

```python
import concourse.bass as bass
from concourse import mybir
from contextlib import ExitStack


def attention_and_experts(nc, x_d, qw_d, kw_d, vw_d, ow_d, gw_d, gb_d,
                          w1s_d, w2s_d, w3s_d, w1r_d, w2r_d, w3r_d, out_d):
    F32, F32R, BF16 = mybir.dt.float32, mybir.dt.float32r, mybir.dt.bfloat16
    ALU, ACT, AX = mybir.AluOpType, mybir.ActivationFunctionType, mybir.AxisListType

    B, S, D = x_d.shape
    HD = kw_d.shape[0]
    NH = D // HD
    NE, _, HID = w1r_d.shape
    TOPK = 4
    P = 128
    N = B * S
    TB = 512
    NTB = N // TB
    TPB = TB // P
    KK = D // P
    G = 4
    NHG = NH // G
    NU = NTB * NHG
    UPB = NU // B
    KT = S // P
    LEVELS = 3
    Q_LEVEL = (0, 0, 0, 1, 1, 2)
    K_LEVEL = (0, 1, 2, 0, 1, 0)
    SLOTS = len(Q_LEVEL)
    SROWS = SLOTS * HD
    MROWS = 2
    QROWS = SROWS + MROWS
    SCALE = float(HD) ** -0.5
    EPS = 1e-5
    PM = 3
    PR = 4
    PL = 32
    PROWS = LEVELS * PL
    NCT = NE * HID // P
    assert NCT * P == NE * HID and NCT % 2 == 0

    x_v = x_d.rearrange("b (t p) d -> p (b t) d", p=P)

    lev_d = nc.dram_tensor("lev_scratch", (NTB, LEVELS, PM * P, TB), BF16).ap()
    wcat_d = nc.dram_tensor("wcat_scratch", (2, D, NE * HID), F32).ap()
    ot_d = nc.dram_tensor("ot_scratch", (P, NU, TB), F32).ap()

    persist = ExitStack()
    with persist:
        def sb(name, shape, dt):
            return persist.enter_context(nc.sbuf_tensor(name, shape, dt))

        def sem(name):
            return persist.enter_context(nc.semaphore(name))

        psum = persist.enter_context(nc.psum_tensor("psum", [P, 8, 512], F32))

        ident = sb("ident", [P, P], F32)
        xhi = sb("xhi", [P, KK, N], F32R)
        xlo = sb("xlo", [P, KK, N], F32R)
        woT = sb("woT", [P, KK, D], F32)
        logits = sb("logits", [P, N // P, NE], F32)
        pl = sb("pl", [P, N // P, PROWS], BF16)
        identb = sb("identb", [P, P], BF16)

        first = ExitStack()
        with first:
            def fb(name, shape, dt):
                return first.enter_context(nc.sbuf_tensor(name, shape, dt))

            x_all = fb("x_all", [P, N // P, D], F32)
            qw_sb = fb("qw_sb", [P, KK, D], F32)
            ow_sb = fb("ow_sb", [P, KK, D], F32)
            kvg_sb = fb("kvg_sb", [3 * HD, D], F32)
            wqkT = fb("wqkT", [P, KK, PM * P], F32)
            wvgT = fb("wvgT", [P, KK, 2 * HD], F32)
            bn6 = fb("bn6", [P, TPB, 6], F32)
            mv = fb("mv", [P, TPB, 2], F32)
            std = fb("std", [P, TPB], F32)
            rstd = fb("rstd", [P, TPB], F32)
            eps = fb("eps", [P, 1], F32)
            guard = fb("guard", [P, 1], F32)
            xn = fb("xn", [P, TPB, D], F32)
            xt = fb("xt", [P, KK, TB], F32)
            lev = fb("lev", [P, LEVELS, PM * TB], BF16)
            r1 = fb("r1", [P, PM * TB], F32)
            qst = fb("qst", [QROWS, NU, G, TB], BF16)
            kst = fb("kst", [QROWS, N], BF16)
            vext = fb("vext", [P, N // P, 32], F32)
            probs = fb("probs", [P, PR, G, TB], F32)
            mx = fb("mx", [P, TPB * G], F32)
            mneg = fb("mneg", [P, TPB, MROWS, G], BF16)
            mT = fb("mT", [MROWS * G, TB], BF16)
            ot = fb("ot", [P, TB], F32)
            gb = fb("gb", [P, NE], F32)

            NT = N // P

            def carve(at, *shape):
                size = 1
                for n in shape:
                    size *= n
                a = r1[:, at:at + size]
                return (a.rearrange("p (t e) -> p t e", t=shape[0]) if len(shape) == 2 else a), at + size

            score, at = carve(0, NT, NE)
            weight, at = carve(at, NT, NE)
            above, at = carve(at, NT, NE)
            equal, at = carve(at, NT, NE)
            top8, at = carve(at, NT, 8)
            total, at = carve(at, NT)
            assert at <= PM * TB
            runs = [xn[:, 2 * i:2 * i + 2, :].rearrange("p j d -> p (j d)")[:, 0:NT * (NE // 2 + NE)]
                    .rearrange("p (t e) -> p t e", t=NT) for i in range(2)]

            wload = sem("wload")
            xload0 = sem("xload0")
            xload = sem("xload")
            consts = sem("consts")
            identbs = sem("identbs")
            wtp = sem("wtp")
            wev = sem("wev")
            lnc = sem("lnc")
            stats = sem("stats")
            stdv = sem("stdv")
            xnr = sem("xnr")
            xtp = sem("xtp")
            xtr = sem("xtr")
            xhs = sem("xhs")
            xsp = sem("xsp")
            proj = sem("proj")
            qhs = sem("qhs")
            r1s = sem("r1s")
            qms = sem("qms")
            qls = sem("qls")
            gbld = sem("gbld")
            sgs = sem("sgs")
            rts = sem("rts")
            rws = sem("rws")
            pls = sem("pls")
            relay = sem("relay")
            vgs = sem("vgs")
            levst = sem("levst")
            qkld = sem("qkld")
            mxp = sem("mxp")
            mxd = sem("mxd")
            nhs = sem("nhs")
            mns = sem("mns")
            mrow = sem("mrow")
            sps = sem("sps")
            spe = sem("spe")
            avs = sem("avs")
            ots = sem("ots")
            otst = sem("otst")

            RING = 3
            AVB = 3
            MXB = 4
            TR_KT = 5
            PER_U = KT * G + 1
            assert PER_U % RING == 0
            NMX = TPB * G
            PV_LAG = 2
            LAST = NU - 1

            def ring_pos(u, kt, h):
                late = 1 if kt >= TR_KT and not (isinstance(u, int) and u == LAST) else 0
                return 1 + kt * G + h + late

            def ring_tr(u):
                return u * PER_U + 1 + TR_KT * G

            def ring_use(u, kt, h):
                return u * PER_U + ring_pos(u, kt, h)

            def started(u):
                return not (isinstance(u, int) and u == 0)

            with nc.Block() as block:

                @block.sync
                def _(sp):
                    sp.dma_start(x_all[:, 0:TPB, :], x_v[:, 0:TPB, :]).then_inc(xload0, 16)
                    sp.dma_start(qw_sb[:, :, :], qw_d.rearrange("(a p) d -> p a d", p=P)).then_inc(wload, 16)
                    sp.dma_start(kvg_sb[0:HD, :], kw_d).then_inc(wload, 16)
                    sp.dma_start(kvg_sb[HD:2 * HD, :], vw_d).then_inc(wload, 16)
                    sp.dma_start(kvg_sb[2 * HD:3 * HD, :], gw_d).then_inc(wload, 16)
                    sp.dma_start(ow_sb[:, :, :], ow_d.rearrange("(a p) d -> p a d", p=P)).then_inc(wload, 16)
                    sp.dma_start(x_all[:, TPB:, :], x_v[:, TPB:, :]).then_inc(xload, 16)
                    sp.dma_start(gb[:, :], gb_d.partition_broadcast(P)).then_inc(gbld, 16)

                    def stack_parts(tb):
                        sp.wait_ge(qls, tb + 1)
                        for lv in range(LEVELS):
                            if lv == 1 and started(tb):
                                sp.wait_ge(qkld, tb * (2 * SLOTS * 16))
                            sp.dma_start(lev_d[bass.ds(tb, 1), lv].rearrange("a (m p) q -> p (a m) q", p=P),
                                         lev[:, lv, :].rearrange("p (m q) -> p m q", m=PM)).then_inc(levst, 16)
                        sp.wait_ge(levst, (tb + 1) * (16 * LEVELS))
                        for s in range(SLOTS):
                            sp.dma_start(qst[s * HD:(s + 1) * HD, bass.ds(tb * NHG, NHG), :, :]
                                         .rearrange("d u g q -> d (u g) q"),
                                         lev_d[bass.ds(tb, 1), Q_LEVEL[s], 0:D].rearrange("a (n d) q -> d (a n) q", d=HD)
                                         ).then_inc(qkld, 16)
                            sp.dma_start(kst[s * HD:(s + 1) * HD, bass.ds(tb * TB, TB)],
                                         lev_d[bass.ds(tb, 1), K_LEVEL[s], D:D + HD].rearrange("a d q -> d (a q)")
                                         ).then_inc(qkld, 16)

                    stack_parts(0)
                    with sp.Fori(1, NTB) as tb:
                        stack_parts(tb)
                    for m, w in enumerate((w1r_d, w3r_d)):
                        sp.dma_start(wcat_d[m].rearrange("d (e c) -> e d c", e=NE), w).then_inc(relay, 16)

                    def put_max(u):
                        for lv in range(MROWS):
                            sp.dma_start(qst[SROWS + lv:SROWS + lv + 1, bass.ds(u, 1), :, :]
                                         .rearrange("l u g q -> l (u g) q"),
                                         mT[lv * G:(lv + 1) * G, :]).then_inc(mrow, 16)

                    def store_ot(u):
                        sp.dma_start(ot_d[:, bass.ds(u, 1), :].rearrange("p u q -> p (u q)"),
                                     ot[:, :]).then_inc(otst, 16)

                    sp.wait_ge(spe, 1)
                    put_max(0)
                    sp.wait_ge(spe, ring_tr(0) + 1)
                    put_max(1)
                    with sp.Fori(1, LAST) as u:
                        sp.wait_ge(ots, u)
                        store_ot(u - 1)
                        sp.wait_ge(spe, ring_tr(u) + 1)
                        put_max(u + 1)
                    for u in (LAST, NU):
                        sp.wait_ge(ots, u)
                        store_ot(u - 1)
                    sp.wait_ge(otst, 16 * NU)
                    sp.wait_ge(relay, 2 * 16)
                    sp.wait_ge(gbld, 16)

                @block.gpsimd
                def _(pool):
                    g = nc.gpsimd
                    g.memset(ident[:, :], 0.0).then_inc(consts, 1)
                    pool.wait_ge(consts, 1)
                    g.affine_select(out=ident[:, :], in_=ident[:, :], compare_op=ALU.not_equal, fill=1.0,
                                    base=0, pattern=[[-1, P]], channel_multiplier=1).then_inc(consts, 1)
                    g.memset(wqkT[:, :, :], 0.0).then_inc(consts, 1)
                    g.memset(vext[:, :, :], 0.0).then_inc(consts, 1)
                    pool.wait_ge(consts, 4)
                    g.memset(vext[:, :, HD:HD + 1], 1.0).then_inc(consts, 1)
                    pool.wait_ge(consts, 5)
                    g.memset(kst[SROWS:QROWS, :], 1.0).then_inc(consts, 1)
                    pool.wait_ge(consts, 6)

                    def split(tb):
                        pool.wait_ge(xtr, tb + 1)
                        if started(tb):
                            pool.wait_ge(xsp, tb)
                        g.tensor_copy(xhi[:, :, bass.ds(tb * TB, TB)], xt[:, :, :]).then_inc(xhs, 1)
                        pool.wait_ge(xhs, tb + 1)
                        g.tensor_tensor(xlo[:, :, bass.ds(tb * TB, TB)], xt[:, :, :],
                                        xhi[:, :, bass.ds(tb * TB, TB)].bitcast(F32), ALU.subtract).then_inc(xsp, 1)

                    split(0)
                    with pool.Fori(1, NTB) as tb:
                        split(tb)

                    pool.wait_ge(xsp, NTB)
                    g.memset(pl[:, :, :], 0.0).then_inc(pls, 1)
                    pool.wait_ge(pls, 1)
                    pool.wait_ge(rws, 1)
                    for lv in range(LEVELS):
                        part = pl[:, :, lv * PL:lv * PL + NE]
                        g.tensor_copy(part, weight[:, :, :]).then_inc(pls, 1)
                        pool.wait_ge(pls, 2 + 2 * lv)
                        if lv < LEVELS - 1:
                            g.tensor_tensor(weight[:, :, :], weight[:, :, :], part, ALU.subtract).then_inc(pls, 1)
                            pool.wait_ge(pls, 3 + 2 * lv)

                @block.vector
                def _(ve):
                    v = nc.vector
                    v.memset(eps[:, :], EPS).then_inc(identbs, 1)
                    ve.wait_ge(consts, 2)
                    v.tensor_copy(identb[:, :], ident[:, :]).then_inc(identbs, 1)

                    def layernorm(tb):
                        for j in range(TPB):
                            src = x_all[:, bass.ds(tb * TPB + j, 1), :].rearrange("p a d -> p (a d)")
                            last = v.bn_stats(bn6[:, j, :], src)
                        last.then_inc(lnc, 1)
                        ve.wait_ge(lnc, tb * 2 + 1)
                        v.memset(guard[:, :], 0.0)
                        for j in range(TPB):
                            last = v.bn_aggr(mv[:, j, :], bn6[:, j, :])
                        last.then_inc(stats, 1)
                        ve.wait_ge(stdv, tb + 1)
                        v.reciprocal(rstd[:, :], std[:, :]).then_inc(lnc, 1)
                        ve.wait_ge(lnc, tb * 2 + 2)
                        if started(tb):
                            ve.wait_ge(xtp, tb)
                        for j in range(TPB):
                            src = x_all[:, bass.ds(tb * TPB + j, 1), :].rearrange("p a d -> p (a d)")
                            last = v.tensor_scalar(xn[:, j, :], src, mv[:, j, 0:1], rstd[:, j:j + 1],
                                                   ALU.subtract, ALU.mult)
                        last.then_inc(xnr, 1)

                    def parts(tb):
                        ve.wait_ge(proj, tb + 1)
                        ve.wait_ge(qhs, tb + 1)
                        v.tensor_tensor(r1[:, :], psum[:, 2:2 + PM, :].rearrange("p m q -> p (m q)"),
                                        lev[:, 0, :], ALU.subtract).then_inc(r1s, 1)
                        vg = psum[:, 5, 0:TPB * 2 * HD].rearrange("p (j c) -> p j c", j=TPB)
                        v.tensor_copy(vext[:, bass.ds(tb * TPB, TPB), 0:HD], vg[:, :, 0:HD])
                        v.tensor_copy(logits[:, bass.ds(tb * TPB, TPB), :], vg[:, :, HD:2 * HD]).then_inc(vgs, 1)
                        ve.wait_ge(qms, tb + 1)
                        if started(tb):
                            ve.wait_ge(levst, tb * (16 * LEVELS))
                        v.tensor_tensor(lev[:, 2, :], r1[:, :], lev[:, 1, :], ALU.subtract).then_inc(qls, 1)

                    ve.wait_ge(xload0, 16)
                    layernorm(0)
                    ve.wait_ge(xload, 16)
                    ve.wait_ge(consts, 5)
                    layernorm(1)
                    parts(0)
                    with ve.Fori(1, NTB - 1) as tb:
                        layernorm(tb + 1)
                        parts(tb)
                    parts(NTB - 1)

                    done = [0]

                    def step(ins):
                        done[0] += 1
                        ins.then_inc(rts, 1)
                        ve.wait_ge(rts, done[0])

                    every = [P, NT, NE]
                    ve.wait_ge(gbld, 16)
                    ve.wait_ge(sgs, 1)
                    step(v.tensor_tensor(score[:, :, :], score[:, :, :], gb[:, :].unsqueeze(1).broadcast_to(every), ALU.add))
                    for i in range(NT):
                        last = v.max(top8[:, i, :], score[:, i, :])
                    step(last)
                    least = top8[:, :, TOPK - 1:TOPK].broadcast_to(every)
                    count = [run[:, :, NE // 2:] for run in runs]
                    v.memset(runs[0][:, :, 0:NE // 2], 0.0)
                    v.memset(runs[1][:, :, 0:NE // 2], 0.0)
                    v.tensor_tensor(above[:, :, :], score[:, :, :], least, ALU.is_gt)
                    v.tensor_tensor(equal[:, :, :], score[:, :, :], least, ALU.is_equal)
                    step(v.tensor_tensor(count[0], score[:, :, :], least, ALU.is_equal))
                    shift, at = 1, 0
                    while shift < NE:
                        lo = NE // 2 - shift
                        step(v.tensor_tensor(count[1 - at], count[at], runs[at][:, :, lo:lo + NE], ALU.add))
                        shift, at = 2 * shift, 1 - at
                    step(v.tensor_reduce(total[:, :], above[:, :, :], AX.X, ALU.add))
                    step(v.tensor_tensor(count[at], count[at], total[:, :].unsqueeze(2).broadcast_to(every), ALU.add))
                    step(v.scalar_tensor_tensor(equal[:, :, :], count[at], float(TOPK), equal[:, :, :],
                                                ALU.is_le, ALU.mult))
                    step(v.tensor_tensor(above[:, :, :], above[:, :, :], equal[:, :, :], ALU.add))
                    step(v.tensor_tensor(weight[:, :, :], above[:, :, :], score[:, :, :], ALU.mult))
                    step(v.tensor_reduce(total[:, :], weight[:, :, :], AX.X, ALU.add))
                    step(v.reciprocal(total[:, :], total[:, :]))
                    v.tensor_tensor(weight[:, :, :], weight[:, :, :], total[:, :].unsqueeze(2).broadcast_to(every),
                                    ALU.mult).then_inc(rws, 1)

                    def unit_maxima(u):
                        for i in range(NMX):
                            ve.wait_ge(mxp, u * NMX + (i + 1))
                            b0 = MXB + 2 * (i % 2)
                            if i == 0 and started(u):
                                ve.wait_ge(mns, u)
                            v.tensor_reduce(mx[:, i:i + 1], psum[:, b0:b0 + 2, :].rearrange("p b k -> p (b k)"),
                                            AX.X, ALU.max).then_inc(mxd, 1)
                        ve.wait_ge(mxd, u * NMX + NMX)
                        if started(u):
                            ve.wait_ge(sps, 1 if isinstance(u, int) and u == 1 else ring_tr(u - 2) + 1)
                        m = mx[:, :].rearrange("p (t g) -> p t g", t=TPB)
                        v.tensor_scalar(mneg[:, :, 0, :], m, -1.0, None, ALU.mult).then_inc(nhs, 1)
                        ve.wait_ge(nhs, u + 1)
                        v.scalar_tensor_tensor(mneg[:, :, 1, :], m, -1.0, mneg[:, :, 0, :],
                                               ALU.mult, ALU.subtract).then_inc(mns, 1)

                    unit_maxima(0)
                    unit_maxima(1)
                    with ve.Fori(2, NU) as u:
                        unit_maxima(u)

                @block.scalar
                def _(act):
                    s = nc.scalar
                    act.wait_ge(identbs, 1)
                    act.wait_ge(stats, 1)
                    s.activation(std[:, :], mv[:, :, 1], ACT.Sqrt, bias=eps[:, :]).then_inc(stdv, 1)
                    act.wait_ge(consts, 3)
                    act.wait_ge(wtp, 1)
                    s.copy(wqkT[:, :, 0:D], psum[:, 0, :].rearrange("p (a d) -> p a d", a=KK)).then_inc(wev, 1)
                    kvg = psum[:, 5, 0:KK * 3 * HD].rearrange("p (a c) -> p a c", a=KK)
                    s.copy(wqkT[:, :, D:D + HD], kvg[:, :, 0:HD]).then_inc(wev, 1)
                    s.copy(wvgT[:, :, :], kvg[:, :, HD:3 * HD]).then_inc(wev, 1)
                    s.copy(woT[:, :, :], psum[:, 1, :].rearrange("p (a d) -> p a d", a=KK)).then_inc(wev, 1)

                    def block_parts(tb, more):
                        act.wait_ge(xtp, tb + 1)
                        if started(tb):
                            act.wait_ge(proj, tb)
                            act.wait_ge(xsp, tb)
                        s.copy(xt[:, :, :], psum[:, 0:KK, :]).then_inc(xtr, 1)
                        if more:
                            act.wait_ge(stats, tb + 2)
                            s.activation(std[:, :], mv[:, :, 1], ACT.Sqrt, bias=eps[:, :]).then_inc(stdv, 1)
                        act.wait_ge(proj, tb + 1)
                        if started(tb):
                            act.wait_ge(levst, tb * (16 * LEVELS))
                        s.copy(lev[:, 0, :], psum[:, 2:2 + PM, :].rearrange("p m q -> p (m q)")).then_inc(qhs, 1)
                        act.wait_ge(r1s, tb + 1)
                        s.copy(lev[:, 1, :], r1[:, :]).then_inc(qms, 1)

                    block_parts(0, True)
                    with act.Fori(1, NTB - 1) as tb:
                        block_parts(tb, True)
                    block_parts(NTB - 1, False)

                    act.wait_ge(qls, NTB)
                    act.wait_ge(vgs, NTB)
                    s.activation(score[:, :, :], logits[:, :, :], ACT.Sigmoid).then_inc(sgs, 1)

                    def move_max(u, use, bank):
                        act.wait_ge(sps, use + 1)
                        if started(u):
                            act.wait_ge(mrow, u * (16 * MROWS))
                        s.copy(mT[:, :], psum[0:MROWS * G, bank, :].bitcast(BF16)[:, 0:TB]).then_inc(spe, 1)

                    def exps(u, last=False):
                        for kt in range(KT):
                            if kt == TR_KT and not last:
                                move_max(u + 1, ring_tr(u), (1 + TR_KT * G) % RING)
                            for h in range(G):
                                act.wait_ge(sps, ring_use(u, kt, h) + 1)
                                if h == 0 and (started(u) or kt >= PR):
                                    act.wait_ge(avs, u * KT + (kt - PR + 1))
                                s.activation(probs[:, kt % PR, h, :], psum[:, ring_pos(u, kt, h) % RING, :],
                                             ACT.Exp, bias=0.0, scale=SCALE).then_inc(spe, 1)
                                if kt == PV_LAG and h == 0 and started(u):
                                    out_unit(u - 1)

                    def out_unit(u):
                        act.wait_ge(avs, (u + 1) * KT)
                        if started(u):
                            act.wait_ge(otst, u * 16)
                        s.copy(ot[:, :], psum[:, AVB, :]).then_inc(ots, 1)

                    move_max(0, 0, 0)
                    exps(0)
                    exps(1)
                    with act.Fori(2, LAST) as u:
                        exps(u)
                    exps(LAST, last=True)
                    out_unit(LAST)

                @block.tensor
                def _(pe):
                    t = nc.tensor
                    pe.wait_ge(consts, 2)
                    pe.wait_ge(wload, 5 * 16)
                    for a in range(KK):
                        for k in range(KK):
                            c = k * D + a * P
                            t.transpose(psum[:, 0, c:c + P], qw_sb[:, a, k * P:(k + 1) * P], ident[:, :])
                            t.transpose(psum[:, 1, c:c + P], ow_sb[:, a, k * P:(k + 1) * P], ident[:, :])
                    for k in range(KK):
                        last = t.transpose(psum[:, 5, k * 3 * HD:(k + 1) * 3 * HD], kvg_sb[:, k * P:(k + 1) * P],
                                           ident[0:3 * HD, 0:3 * HD])
                    last.then_inc(wtp, 1)
                    pe.wait_ge(wev, 4)

                    def project(tb):
                        pe.wait_ge(xnr, tb + 1)
                        if started(tb):
                            pe.wait_ge(xtr, tb)
                        for k in range(KK):
                            for j in range(TPB):
                                last = t.transpose(psum[:, k, j * P:(j + 1) * P], xn[:, j, k * P:(k + 1) * P],
                                                   ident[:, :])
                        last.then_inc(xtp, 1)
                        pe.wait_ge(xtr, tb + 1)
                        if started(tb):
                            pe.wait_ge(r1s, tb)
                            pe.wait_ge(vgs, tb)
                        for j in range(TPB):
                            for k in range(KK):
                                t.matmul(psum[:, 5, j * 2 * HD:(j + 1) * 2 * HD], xt[:, k, j * P:(j + 1) * P],
                                         wvgT[:, k, :], start=(k == 0), stop=(k == KK - 1))
                        for m in range(PM):
                            for k in range(KK):
                                last = t.matmul(psum[:, 2 + m, :], wqkT[:, k, m * P:(m + 1) * P], xt[:, k, :],
                                                start=(k == 0), stop=(k == KK - 1))
                        last.then_inc(proj, 1)

                    project(0)
                    with pe.Fori(1, NTB) as tb:
                        project(tb)

                    def score_max(u, i, half, batch):
                        q0 = i // G * P
                        if half == 0 and (started(u) or i >= 2):
                            pe.wait_ge(mxd, u * NMX + (i - 1))
                        k0 = batch * S + half * 512
                        ins = t.matmul(psum[:, MXB + 2 * (i % 2) + half, :],
                                       qst[0:SROWS, bass.ds(u, 1), i % G, q0:q0 + P].rearrange("r u q -> r (u q)"),
                                       kst[0:SROWS, k0:k0 + 512], start=True, stop=True)
                        if half == 1:
                            ins.then_inc(mxp, 1)

                    def transpose_max(u, use, pos):
                        pe.wait_ge(mns, u + 1)
                        if use is not None:
                            pe.wait_ge(spe, use - RING + 1)
                        view = psum[0:MROWS * G, pos % RING, :].bitcast(BF16)
                        for j in range(TPB):
                            last = t.transpose(view[:, j * P:(j + 1) * P],
                                               mneg[:, j, :, :].rearrange("p l g -> p (l g)"), identb[:, :])
                        last.then_inc(sps, 1)

                    def scores(u, kt, h, batch):
                        use = ring_use(u, kt, h)
                        if started(u) or use >= RING:
                            pe.wait_ge(spe, use - RING + 1)
                        k0 = batch * S + kt * P
                        t.matmul(psum[:, ring_pos(u, kt, h) % RING, :], kst[:, k0:k0 + P],
                                 qst[:, bass.ds(u, 1), h, :].rearrange("r u q -> r (u q)"),
                                 start=True, stop=True).then_inc(sps, 1)

                    def pv(u, kt, batch):
                        pe.wait_ge(spe, ring_use(u, kt, G - 1) + 1)
                        if kt == 0 and started(u):
                            pe.wait_ge(ots, u)
                        for h in range(G):
                            last = t.matmul(psum[32 * h:32 * h + 32, AVB, :], vext[:, batch * KT + kt, :],
                                            probs[:, kt % PR, h, :], start=(kt == 0), stop=(kt == KT - 1),
                                            tile_position=(0, 32 * h))
                        last.then_inc(avs, 1)

                    HALF = KT // 2

                    def unit(u, batch, before, after, after2):
                        pe.wait_ge(mrow, (u + 1) * (16 * MROWS))
                        for kt in range(KT):
                            if kt == TR_KT and after is not None:
                                transpose_max(u + 1, ring_tr(u), 1 + TR_KT * G)
                            for h in range(G):
                                scores(u, kt, h, batch)
                                i = (NMX // 2 + 2 * kt if kt < HALF else 2 * (kt - HALF)) + h // 2
                                if kt < HALF and after is not None:
                                    score_max(u + 1, i, h % 2, after)
                                if kt >= HALF and after2 is not None:
                                    score_max(u + 2, i, h % 2, after2)
                            if kt >= PV_LAG:
                                pv(u, kt - PV_LAG, batch)
                            elif started(u):
                                pv(u - 1, KT - PV_LAG + kt, before)

                    pe.wait_ge(qhs, NTB)
                    pe.wait_ge(r1s, NTB)
                    pe.wait_ge(vgs, NTB)
                    pe.wait_ge(consts, 6)
                    pe.wait_ge(identbs, 2)
                    pe.wait_ge(qkld, NTB // B * 2 * SLOTS * 16)
                    for i in range(NMX):
                        for half in range(2):
                            score_max(0, i, half, 0)
                    for i in range(NMX // 2):
                        for half in range(2):
                            score_max(1, i, half, 0)
                    transpose_max(0, None, 0)
                    unit(0, 0, None, 0, 0)
                    with pe.Fori(1, UPB - 2) as u:
                        unit(u, 0, 0, 0, 0)
                    pe.wait_ge(qkld, NTB * 2 * SLOTS * 16)
                    unit(UPB - 2, 0, 0, 0, 1)
                    unit(UPB - 1, 0, 0, 1, 1)
                    unit(UPB, 1, 0, 1, 1)
                    with pe.Fori(UPB + 1, NU - 2) as u:
                        unit(u, 1, 1, 1, 1)
                    unit(NU - 2, 1, 1, 1, None)
                    unit(NU - 1, 1, 1, None, None)
                    for kt in range(KT - PV_LAG, KT):
                        pv(NU - 1, kt, 1)

        second = ExitStack()
        with second:
            def sb2(name, shape, dt):
                return second.enter_context(nc.sbuf_tensor(name, shape, dt))

            raw13 = [sb2(f"raw13_{i}", [P, 2, KK, 2 * P], F32) for i in range(2)]
            raw2 = [sb2(f"raw2_{i}", [P, 2, D], F32) for i in range(2)]
            w13 = [[sb2(f"w13_{i}_{q}", [P, 2, KK, 2 * P], F32R) for q in range(2)] for i in range(2)]
            w2 = [[sb2(f"w2_{i}_{q}", [P, 2, D], F32R) for q in range(2)] for i in range(2)]
            select = sb2("select", [PROWS, NCT * P], BF16)
            pT = sb2("pT", [PROWS, N], BF16)
            h1c = [sb2(f"h1c_{i}", [P, TB], F32) for i in range(2)]
            prod = [sb2(f"prod_{i}", [P, TB], F32) for i in range(2)]
            gate = [sb2(f"gate_{i}", [P, TB], F32) for i in range(2)]
            hid = [sb2(f"hid_{i}", [P, TB], F32) for i in range(2)]
            hidp = [[sb2(f"hidp_{i}_{q}", [P, TB], F32R) for q in range(2)] for i in range(2)]
            acc = sb2("acc", [P, KK, N], F32)
            ots_sb = [sb2(f"ots_sb_{i}", [P, NHG, TB], F32) for i in range(2)]
            xs = [sb2(f"xs_{i}", [P, TPB, D], F32) for i in range(2)]
            rsum = [sb2(f"rsum_{i}", [P, NH], F32) for i in range(2)]
            on = [sb2(f"on_{i}", [P, NH, HD], F32) for i in range(2)]
            onT = [sb2(f"onT_{i}", [P, KK, P], F32) for i in range(2)]
            y_sb = [sb2(f"y_sb_{i}", [P, D], F32) for i in range(2)]

            zeroed = sem("zeroed")
            cut = sem("cut")
            sels = sem("sels")
            padded = sem("padded")
            ptp = sem("ptp")
            pts = sem("pts")
            rawld = [sem(f"rawld_{i}") for i in range(2)]
            wsp = sem("wsp")
            h1p = sem("h1p")
            h2p = sem("h2p")
            pbp = sem("pbp")
            h1s = sem("h1s")
            prs = sem("prs")
            gts = sem("gts")
            hds = sem("hds")
            hhs = sem("hhs")
            hls = sem("hls")
            s2p = sem("s2p")
            accd = sem("accd")
            finld = [sem(f"finld_{i}") for i in range(2)]
            otp = sem("otp")
            rcs = sem("rcs")
            ons = sem("ons")
            ontp = sem("ontp")
            onts = sem("onts")
            yp = sem("yp")
            ys = sem("ys")
            yst = [sem(f"yst_{i}") for i in range(2)]

            H1B, H2B, PBB, OB = 0, 2, 4, 6
            NPAIR = NCT // 2 + 1
            SHARED = NPAIR - 1
            STEPS = 2 * NTB
            LAG = 2
            CS = HID - P
            PIECES = 4
            LOADS = 3 * 16
            assert NPAIR % 2 == 0
            PRODUCTS = ((0, 0), (0, 1), (1, 0))

            def pairs(eng, body):
                body(0, 0, 0)
                body(1, 1, 0)
                with eng.Fori(1, NPAIR // 2 - 1) as i:
                    body(i * 2, 0, i)
                    body(i * 2 + 1, 1, i)
                body(NPAIR - 2, 0, NPAIR // 2 - 1)
                body(SHARED, 1, NPAIR // 2 - 1)

            def is_shared(n):
                return isinstance(n, int) and n == SHARED

            def since(n, k, steps):
                return not isinstance(n, int) or n * STEPS + k >= steps

            with nc.Block() as block:

                @block.sync
                def _(sp):
                    def load(n, i):
                        for m in range(2):
                            sp.dma_start(raw13[i][:, m, :, :],
                                         wcat_d[m, :, bass.ds(n * (2 * P), 2 * P)].rearrange("(k p) c -> p k c", p=P)
                                         ).then_inc(rawld[i], 16)
                        w = w2r_d.rearrange("e c d -> (e c) d")
                        sp.dma_start(raw2[i][:, :, :], w[bass.ds(n * (2 * P), 2 * P), :]
                                     .rearrange("(j p) d -> p j d", p=P)).then_inc(rawld[i], 16)

                    load(0, 0)
                    load(1, 1)
                    with sp.Fori(0, (NPAIR - 4) // 2) as i:
                        sp.wait_ge(wsp, i * (2 * PIECES) + PIECES)
                        load(i * 2 + 2, 0)
                        sp.wait_ge(wsp, i * (2 * PIECES) + 2 * PIECES)
                        load(i * 2 + 3, 1)
                    sp.wait_ge(wsp, (NPAIR - 3) * PIECES)
                    load(NPAIR - 2, 0)
                    sp.wait_ge(padded, 2)
                    for m, w in enumerate((w1s_d, w3s_d)):
                        sp.dma_start(raw13[1][:, m, :, 0:HID], w.rearrange("(k p) c -> p k c", p=P)
                                     ).then_inc(rawld[1], 16)
                    sp.dma_start(raw2[1][:, 0, :], w2s_d[0:P, :]).then_inc(rawld[1], 16)
                    sp.dma_start(raw2[1][0:CS, 1, :], w2s_d[P:HID, :]).then_inc(rawld[1], 16)

                    def last_loads(tb):
                        i = tb % 2
                        sp.dma_start(ots_sb[i][:, :, :], ot_d[:, tb * NHG:(tb + 1) * NHG, :]).then_inc(finld[i], 16)
                        sp.dma_start(xs[i][:, :, :], x_v[:, tb * TPB:(tb + 1) * TPB, :]).then_inc(finld[i], 16)

                    out_v = out_d.rearrange("b (t p) d -> p (b t) d", p=P)
                    last_loads(0)
                    last_loads(1)
                    for t in range(NT):
                        sp.wait_ge(ys, t + 1)
                        sp.dma_start(out_v[:, t, :], y_sb[t % 2][:, :]).then_inc(yst[t % 2], 16)
                        if t % TPB == TPB - 1 and t // TPB + 2 < NTB:
                            last_loads(t // TPB + 2)
                    for i in range(2):
                        sp.wait_ge(yst[i], NT // 2 * 16)

                @block.gpsimd
                def _(pool):
                    g = nc.gpsimd
                    rows = select[0:PL, :]
                    pool.wait_ge(zeroed, 1)
                    g.affine_select(out=rows, in_=rows, compare_op=ALU.is_ge, fill=0.0, base=0,
                                    pattern=[[1, NCT * P]], channel_multiplier=-HID).then_inc(cut, 1)
                    pool.wait_ge(cut, 1)
                    g.affine_select(out=rows, in_=rows, compare_op=ALU.is_ge, fill=0.0, base=HID - 1,
                                    pattern=[[-1, NCT * P]], channel_multiplier=HID).then_inc(cut, 1)
                    pool.wait_ge(cut, 2)

                    def split(n, i, piece):
                        raw, part = ((raw13[i], w13[i]), (raw2[i], w2[i]))[piece // 2]
                        dims = "p a b c -> p (a b c)" if piece < 2 else "p a c -> p (a c)"
                        raw, high, low = (a[:].rearrange(dims) for a in (raw, part[0], part[1]))
                        if piece % 2 == 0:
                            g.tensor_copy(high, raw).then_inc(wsp, 1)
                        else:
                            g.tensor_tensor(low, raw, high.bitcast(F32), ALU.subtract).then_inc(wsp, 1)
                        pool.wait_ge(wsp, n * PIECES + (piece + 1))

                    def low_parts(n, i, r):
                        st = n * STEPS
                        for k in range(STEPS):
                            c = k % 2
                            if k == 0 and isinstance(n, int) and n == NPAIR - 2:
                                g.memset(raw13[1][:, :, :, HID:], 0.0).then_inc(padded, 1)
                                g.memset(raw2[1][:, 1, :], 0.0).then_inc(padded, 1)
                            if k == 2 and not is_shared(n):
                                whole = n == NPAIR - 2 if isinstance(n, int) else False
                                pool.wait_ge(rawld[1 - i], (r + i) * LOADS + (4 * 16 if whole else LOADS))
                            pool.wait_ge(hhs, st + (k + 1))
                            if since(n, k, 2):
                                pool.wait_ge(s2p, st + (k - 1))
                            g.tensor_tensor(hidp[c][1][:, :], hid[c][:, :], hidp[c][0][:, :].bitcast(F32),
                                            ALU.subtract).then_inc(hls, 1)
                            if 2 <= k < 2 + PIECES and not is_shared(n):
                                split(n + 1, 1 - i, k - 2)

                    pairs(pool, low_parts)

                @block.vector
                def _(ve):
                    v = nc.vector
                    v.memset(select[0:PL, :], 1.0).then_inc(zeroed, 1)
                    v.memset(acc[:, :, :], 0.0).then_inc(zeroed, 1)
                    ve.wait_ge(wsp, 1)
                    v.tensor_tensor(w13[0][1][:, :, :, :], raw13[0][:, :, :, :], w13[0][0][:, :, :, :].bitcast(F32),
                                    ALU.subtract).then_inc(wsp, 1)
                    ve.wait_ge(wsp, 3)
                    v.tensor_tensor(w2[0][1][:, :, :], raw2[0][:, :, :], w2[0][0][:, :, :].bitcast(F32),
                                    ALU.subtract).then_inc(wsp, 1)
                    ve.wait_ge(cut, 2)
                    for lv in range(1, LEVELS):
                        v.tensor_copy(select[lv * PL:(lv + 1) * PL, :], select[0:PL, :]).then_inc(sels, 1)
                    ve.wait_ge(zeroed, 2)

                    def add_sums(tb, done):
                        ve.wait_ge(s2p, done)
                        a = acc[:, :, tb * TB:(tb + 1) * TB]
                        v.tensor_tensor(a, psum[:, OB:OB + KK, :], a, ALU.add).then_inc(accd, 1)

                    def hidden(n, i, r):
                        st = n * STEPS
                        for k in range(STEPS):
                            c = k % 2
                            ve.wait_ge(h1s, st + (k + 1))
                            ve.wait_ge(h2p, st + (k + 1))
                            if not is_shared(n):
                                if since(n, k, 2):
                                    ve.wait_ge(gts, st + (k - 1))
                                v.tensor_tensor(prod[c][:, :], psum[:, H2B + c, :], h1c[c][:, :],
                                                ALU.mult).then_inc(prs, 1)
                                ve.wait_ge(gts, st + (k + 1))
                                ve.wait_ge(pbp, st + (k + 1))
                            if since(n, k, 2):
                                ve.wait_ge(hls, st + (k - 1))
                            if is_shared(n):
                                v.tensor_tensor(hid[c][:, :], psum[:, H2B + c, :], h1c[c][:, :],
                                                ALU.mult).then_inc(hds, 1)
                            else:
                                v.tensor_tensor(hid[c][:, :], psum[:, PBB + c, :], gate[c][:, :],
                                                ALU.mult).then_inc(hds, 1)
                            if k % 2 and since(n, k, LAG):
                                add_sums((k - LAG) // 2 % NTB, st + (k - LAG + 1))

                    pairs(ve, hidden)
                    add_sums(NTB - 1, NPAIR * STEPS)

                    for t in range(NT + 2):
                        c = t % 2
                        if t < NT:
                            o = psum[:, c, :].rearrange("p (h w) -> p h w", h=NH)
                            ve.wait_ge(otp, t + 1)
                            if t >= 2:
                                ve.wait_ge(ons, t - 1)
                            v.reciprocal(rsum[c][:, :], o[:, :, HD]).then_inc(rcs, 1)
                            ve.wait_ge(rcs, t + 1)
                            if t >= 2:
                                ve.wait_ge(ontp, t - 1)
                            v.tensor_tensor(on[c][:, :, :], o[:, :, 0:HD],
                                            rsum[c][:, :].unsqueeze(2).broadcast_to([P, NH, HD]),
                                            ALU.mult).then_inc(ons, 1)
                        if t >= 2:
                            ve.wait_ge(yp, t - 1)
                            if t >= 4:
                                ve.wait_ge(yst[c], (t // 2 - 1) * 16)
                            v.tensor_tensor(y_sb[c][:, :], psum[:, 4 + c, 0:D],
                                            xs[(t - 2) // TPB % 2][:, (t - 2) % TPB, :], ALU.add).then_inc(ys, 1)

                @block.scalar
                def _(act):
                    s = nc.scalar
                    act.wait_ge(rawld[0], LOADS)
                    s.copy(w13[0][0][:, :, :, :], raw13[0][:, :, :, :]).then_inc(wsp, 1)
                    act.wait_ge(wsp, 2)
                    s.copy(w2[0][0][:, :, :], raw2[0][:, :, :]).then_inc(wsp, 1)
                    act.wait_ge(ptp, 1)
                    s.copy(pT[:, :], psum[0:PROWS, OB:OB + 2, :].rearrange("p b q -> p (b q)").bitcast(BF16)
                           ).then_inc(pts, 1)

                    def hidden(n, i, r):
                        st = n * STEPS
                        for k in range(STEPS):
                            c = k % 2
                            act.wait_ge(h1p, st + (k + 1))
                            if since(n, k, 2):
                                act.wait_ge(hds if is_shared(n) and k >= 2 else prs, st + (k - 1))
                            s.activation(h1c[c][:, :], psum[:, H1B + c, :],
                                         ACT.Silu if is_shared(n) else ACT.Copy).then_inc(h1s, 1)
                            if not is_shared(n):
                                act.wait_ge(prs, st + (k + 1))
                                if since(n, k, 2):
                                    act.wait_ge(hds, st + (k - 1))
                                s.activation(gate[c][:, :], prod[c][:, :], ACT.Silu).then_inc(gts, 1)
                            act.wait_ge(hds, st + (k + 1))
                            if since(n, k, 2):
                                act.wait_ge(s2p, st + (k - 1))
                            s.copy(hidp[c][0][:, :], hid[c][:, :]).then_inc(hhs, 1)

                    pairs(act, hidden)
                    for t in range(NT):
                        act.wait_ge(ontp, t + 1)
                        if t >= 2:
                            act.wait_ge(yp, t - 1)
                        s.copy(onT[t % 2][:, :, :], psum[:, 2 + t % 2, 0:D].rearrange("p (k q) -> p k q", k=KK)
                               ).then_inc(onts, 1)

                @block.tensor
                def _(pe):
                    t = nc.tensor
                    for j in range(NT):
                        view = psum[0:PROWS, OB + j // 8, :].bitcast(BF16)
                        last = t.transpose(view[:, j % 8 * P:(j % 8 + 1) * P], pl[:, j, :], identb[:, :])
                    last.then_inc(ptp, 1)

                    def first_products(n, i, k):
                        st = n * STEPS
                        c, tb, j = k % 2, k // 2, k % 2
                        if k == 0:
                            pe.wait_ge(wsp, n * PIECES + PIECES)
                        for m, (bank, full) in enumerate(((H1B, h1p), (H2B, h2p))):
                            if since(n, k, 2):
                                pe.wait_ge(h1s if m == 0 else hds if is_shared(n) and k >= 2 else prs, st + (k - 1))
                            for kk in range(KK):
                                for q, (wq, xq) in enumerate(PRODUCTS):
                                    x = (xhi, xlo)[xq][:, kk, tb * TB:(tb + 1) * TB]
                                    last = t.matmul(psum[:, bank + c, :], w13[i][wq][:, m, kk, j * P:(j + 1) * P], x,
                                                    start=(kk == 0 and q == 0), stop=(kk == KK - 1 and q == 2))
                            last.then_inc(full, 1)
                        if not is_shared(n):
                            if since(n, k, 2):
                                pe.wait_ge(hds, st + (k - 1))
                            if isinstance(n, int) and n == 0 and k == 0:
                                pe.wait_ge(pts, 1)
                                pe.wait_ge(sels, 2)
                            t.matmul(psum[:, PBB + c, :], select[:, bass.ds(n * (2 * P) + j * P, P)],
                                     pT[:, tb * TB:(tb + 1) * TB], start=True, stop=True).then_inc(pbp, 1)

                    def second_products(n, i, k):
                        st = n * STEPS
                        c, tb, j = k % 2, k // 2, k % 2
                        pe.wait_ge(hls, st + (k + 1))
                        if j == 0 and since(n, k, 2):
                            pe.wait_ge(accd, n * NTB + tb)
                        for d in range(KK):
                            for q, (wq, hq) in enumerate(PRODUCTS):
                                last = t.matmul(psum[:, OB + d, :], w2[i][wq][:, j, d * P:(d + 1) * P],
                                                hidp[c][hq][:, :], start=(j == 0 and q == 0), stop=(j == 1 and q == 2))
                        last.then_inc(s2p, 1)

                    def pair(n, i, r):
                        for k in range(STEPS):
                            first_products(n, i, k)
                            if k >= LAG:
                                second_products(n, i, k - LAG)
                            elif since(n, k, LAG):
                                second_products(n - 1, 1 - i, STEPS - LAG + k)

                    pairs(pe, pair)
                    for k in range(STEPS - LAG, STEPS):
                        second_products(SHARED, 1, k)

                    pe.wait_ge(h1s, NPAIR * STEPS)
                    pe.wait_ge(hds, NPAIR * STEPS)
                    for n in range(NT + 2):
                        if n < NT:
                            tb, j = n // TPB, n % TPB
                            if j == 0:
                                pe.wait_ge(finld[tb % 2], (tb // 2 + 1) * 32)
                            if n >= 2:
                                pe.wait_ge(ons, n - 1)
                            for h in range(NHG):
                                last = t.transpose(psum[:, n % 2, h * P:(h + 1) * P],
                                                   ots_sb[tb % 2][:, h, j * P:(j + 1) * P], ident[:, :])
                            last.then_inc(otp, 1)
                        m = n - 1
                        if 0 <= m < NT:
                            pe.wait_ge(ons, m + 1)
                            if m >= 2:
                                pe.wait_ge(onts, m - 1)
                            o = on[m % 2][:, :, :].rearrange("p h d -> p (h d)")
                            for k in range(KK):
                                last = t.transpose(psum[:, 2 + m % 2, k * P:(k + 1) * P], o[:, k * P:(k + 1) * P],
                                                   ident[:, :])
                            last.then_inc(ontp, 1)
                        m = n - 2
                        if 0 <= m < NT:
                            pe.wait_ge(onts, m + 1)
                            if m == 0:
                                pe.wait_ge(accd, NPAIR * NTB)
                            if m >= 2:
                                pe.wait_ge(ys, m - 1)
                            y = psum[:, 4 + m % 2, 0:D]
                            for k in range(KK):
                                t.matmul(y, onT[m % 2][:, k, :], woT[:, k, :], start=(k == 0), stop=False)
                            for d in range(KK):
                                last = t.matmul(y[:, d * P:(d + 1) * P], acc[:, d, m * P:(m + 1) * P], ident[:, :],
                                                start=False, stop=(d == KK - 1))
                            last.then_inc(yp, 1)


_INS = ['L0_attn_x', 'L0_attn_q_w', 'L0_attn_k_w', 'L0_attn_v_w', 'L0_attn_o_w', 'L0_ffn_gate_w', 'L0_ffn_gate_b',
        'L0_ffn_w1_shared', 'L0_ffn_w2_shared', 'L0_ffn_w3_shared', 'L0_ffn_w1_routed', 'L0_ffn_w2_routed',
        'L0_ffn_w3_routed']


_OUTS = [((2, 1024, 256), 'float32')]


def kernel(**inputs):
    import numpy as _np
    import concourse.bacc as _bacc
    from concourse import mybir as _mybir
    from concourse.bass_utils import run_bass_kernel_spmd as _run

    nc = _bacc.Bacc("TRN2", target_bir_lowering=False, num_devices=1)
    arrays, args = {}, []
    for name in _INS:
        a = _np.ascontiguousarray(inputs[name])
        arrays[f"in_{name}_dram"] = a
        args.append(nc.dram_tensor(f"in_{name}_dram", a.shape, _mybir.dt.from_np(a.dtype), kind="ExternalInput").ap())
    for i, (shape, dtype) in enumerate(_OUTS):
        dt = _mybir.dt.from_np(_np.dtype(dtype))
        args.append(nc.dram_tensor(f"out_{i}_dram", shape, dt, kind="ExternalOutput").ap())
    attention_and_experts(nc, *args)
    r = _run(nc, [arrays], core_ids=[0])
    return r.results[0]["out_0_dram"]
```
